# Optimizing a Trainium2 kernel written in Bass

```python
import numpy as np
import jax
import jax.numpy as jnp

def _softmax(x, axis=-1):
    return jax.nn.softmax(x, axis=axis)

def _gelu(x):
    return jax.nn.gelu(x, approximate=True)

def _silu(x):
    return jax.nn.silu(x)

def _sigmoid(x):
    return jax.nn.sigmoid(x)

def _layernorm(x, axis=-1, eps=1e-05):
    m = jnp.mean(x, axis=axis, keepdims=True)
    v = jnp.var(x, axis=axis, keepdims=True)
    return (x - m) / jnp.sqrt(v + eps)

def _scatter_add(tgt, idx, src, axis=0):
    return tgt.at[idx].add(src)

def _segment_sum(src, seg, n):
    return jax.ops.segment_sum(src, seg, n)
kernel_name = 'mk_gnn_preln_d2_gnn_r8_deb663'

def setup_inputs(seed: int=0):
    np.random.seed(seed)
    _w = jnp.asarray

    def _rec_inputs():
        import jax
        import jax.numpy as jnp
        _gk = jax.random.key(seed)
        x = -0.0005121 + 1.001 * jax.random.normal(jax.random.fold_in(_gk, 1), (12500, 32), jnp.float32)
        _s = jax.random.randint(jax.random.fold_in(_gk, 2), (200000,), 0, 12500, jnp.int32)
        _d = jax.random.randint(jax.random.fold_in(_gk, 3), (200000,), 0, 12500, jnp.int32)
        _loop = jnp.arange(12500, dtype=jnp.int32)
        src = jnp.concatenate([_s, _d, _loop])
        dst = jnp.concatenate([_d, _s, _loop])
        _o = jnp.argsort(dst, stable=True)
        src = src[_o]
        dst = dst[_o]
        edge_type_86 = jax.random.randint(jax.random.fold_in(_gk, 12), (412500,), 0, 86, jnp.int32)
        return (x, src, dst, edge_type_86)
    x, src, dst, edge_type_86 = _rec_inputs()

    def _L0_gnn_setup():
        import jax, jax.numpy as jnp
        import numpy as np
        N_NODES = 12500
        N_EDGES = 200000
        DIM1 = 32
        LEAKY_SLOPE = 0.01
        key = jax.random.key(seed)
        k1, k2, k3, k4 = jax.random.split(key, 4)
        h = jax.random.normal(k1, (N_NODES, DIM1), dtype=jnp.float32)
        attn_w = jax.random.normal(k2, (2 * DIM1,), dtype=jnp.float32) * (1.0 / np.sqrt(2 * DIM1))
        src = jax.random.randint(k3, (N_EDGES,), 0, N_NODES, dtype=jnp.int32)
        dst = jax.random.randint(k4, (N_EDGES,), 0, N_NODES, dtype=jnp.int32)
        return {'h': h, 'attn_w': attn_w, 'src': src, 'dst': dst}
    _L0_gnn_all = _L0_gnn_setup()
    _L0_gnn_in = {k: v for k, v in _L0_gnn_all.items() if k in ('attn_w',)}
    del _L0_gnn_all

    def _L1_gnn_setup():
        import jax, jax.numpy as jnp
        import numpy as np
        N_NODES = 6250
        N_EDGES = 100000
        INP_DIM = 32
        OUT_DIM = 32
        ATTN_DIM = 32
        NUM_RELS = 86
        NUM_BASES = 16
        GAMMA = 0.0
        key = jax.random.key(seed)
        ks = jax.random.split(key, 12)
        return {'h': jax.random.normal(ks[0], (N_NODES, INP_DIM), jnp.float32), 'weight': jax.random.normal(ks[1], (NUM_BASES, INP_DIM, OUT_DIM), jnp.float32), 'w_comp': jax.random.normal(ks[2], (NUM_RELS, NUM_BASES), jnp.float32), 'self_loop_weight': jax.random.normal(ks[3], (INP_DIM, OUT_DIM), jnp.float32), 'A1_w': jax.random.normal(ks[4], (ATTN_DIM, INP_DIM), jnp.float32), 'A1_b': jax.random.normal(ks[5], (ATTN_DIM,), jnp.float32), 'A2_w': jax.random.normal(ks[6], (ATTN_DIM, INP_DIM), jnp.float32), 'A2_b': jax.random.normal(ks[7], (ATTN_DIM,), jnp.float32), 'rel_emb': jax.random.normal(ks[8], (NUM_RELS, ATTN_DIM), jnp.float32), 'src': jax.random.randint(ks[9], (N_EDGES,), 0, N_NODES, jnp.int32), 'dst': jax.random.randint(ks[10], (N_EDGES,), 0, N_NODES, jnp.int32), 'etype': jax.random.randint(ks[11], (N_EDGES,), 0, NUM_RELS, jnp.int32)}
    _L1_gnn_all = _L1_gnn_setup()
    _L1_gnn_in = {k: v for k, v in _L1_gnn_all.items() if k in ('weight', 'w_comp', 'self_loop_weight', 'A1_w', 'A1_b', 'A2_w', 'A2_b', 'rel_emb')}
    del _L1_gnn_all
    return {'x': x, 'src': src, 'dst': dst, 'edge_type_86': edge_type_86, 'L0_gnn_attn_w': _L0_gnn_in['attn_w'], 'L1_gnn_weight': _L1_gnn_in['weight'], 'L1_gnn_w_comp': _L1_gnn_in['w_comp'], 'L1_gnn_self_loop_weight': _L1_gnn_in['self_loop_weight'], 'L1_gnn_A1_w': _L1_gnn_in['A1_w'], 'L1_gnn_A1_b': _L1_gnn_in['A1_b'], 'L1_gnn_A2_w': _L1_gnn_in['A2_w'], 'L1_gnn_A2_b': _L1_gnn_in['A2_b'], 'L1_gnn_rel_emb': _L1_gnn_in['rel_emb']}

def reference(x, src, dst, edge_type_86, L0_gnn_attn_w, L1_gnn_weight, L1_gnn_w_comp, L1_gnn_self_loop_weight, L1_gnn_A1_w, L1_gnn_A1_b, L1_gnn_A2_w, L1_gnn_A2_b, L1_gnn_rel_emb):
    import jax
    import jax.numpy as jnp

    def _L0_gnn_ref(h, attn_w, src, dst):
        import jax, jax.numpy as jnp
        import numpy as np
        N_NODES = 12500
        N_EDGES = 200000
        DIM1 = 32
        LEAKY_SLOPE = 0.01
        N, d = h.shape
        s_src = h @ attn_w[:d]
        s_dst = h @ attn_w[d:]
        e = s_src[src] + s_dst[dst]
        e = jnp.where(e >= 0, e, LEAKY_SLOPE * e)
        m = jax.ops.segment_max(e, dst, num_segments=N)
        ex = jnp.exp(e - m[dst])
        denom = jax.ops.segment_sum(ex, dst, num_segments=N)
        alpha = ex / denom[dst]
        out = jax.ops.segment_sum(h[src] * alpha[:, None], dst, num_segments=N)
        return out

    def _L1_gnn_ref(h, weight, w_comp, self_loop_weight, A1_w, A1_b, A2_w, A2_b, rel_emb, src, dst, etype):
        import jax, jax.numpy as jnp
        import numpy as np
        N_NODES = 6250
        N_EDGES = 100000
        INP_DIM = 32
        OUT_DIM = 32
        ATTN_DIM = 32
        NUM_RELS = 86
        NUM_BASES = 16
        GAMMA = 0.0
        E = src.shape[0]
        N = h.shape[0]
        x = h[src]
        y = h[dst]
        c = w_comp[etype]
        xb = jnp.einsum('ei,bio->ebo', x, weight)
        msg = jnp.einsum('eb,ebo->eo', c, xb)
        x_hat = x @ A1_w.T + A1_b
        y_hat = y @ A2_w.T + A2_b + rel_emb[etype]
        scale = jnp.sqrt(jnp.asarray(INP_DIM, h.dtype))
        a = jnp.tanh(jax.nn.relu(jnp.sum(x_hat * y_hat, axis=-1) / scale))
        a = jnp.where(a > GAMMA, a, jnp.zeros_like(a))
        nei = jax.ops.segment_sum(a[:, None] * msg, dst, num_segments=N)
        last_e = jax.ops.segment_max(jnp.arange(E, dtype=jnp.int32), dst, num_segments=N)
        last_e = jnp.clip(last_e, 0, E - 1)
        curr = h[src[last_e]] @ self_loop_weight
        in_deg = jax.ops.segment_sum(jnp.ones((E,), h.dtype), dst, num_segments=N)
        h_new = jnp.where((in_deg > 0)[:, None], nei + curr, jnp.zeros_like(nei))
        return jax.nn.relu(h_new)
    h = jnp.maximum(_layernorm(x, axis=-1), 0.0)
    x = x + _L0_gnn_ref(h, L0_gnn_attn_w, src, dst)
    h = jnp.maximum(_layernorm(x, axis=-1), 0.0)
    x = x + _L1_gnn_ref(h, L1_gnn_weight, L1_gnn_w_comp, L1_gnn_self_loop_weight, L1_gnn_A1_w, L1_gnn_A1_b, L1_gnn_A2_w, L1_gnn_A2_b, L1_gnn_rel_emb, src, dst, edge_type_86)
    return x

_drawn_inputs = setup_inputs


def setup_inputs(seed=0):
    import zlib

    import numpy as np

    out = dict(_drawn_inputs(seed))
    spreads = {}
    factors = {}
    for name, (base, spread) in spreads.items():
        noise = np.random.default_rng([zlib.crc32(name.encode()), seed]).standard_normal(out[name].shape)
        drawn = base * np.exp(spread * noise) if base else spread * noise
        out[name] = jnp.asarray(drawn.astype(out[name].dtype))
    for name, factor in factors.items():
        out[name] = (out[name] * factor).astype(out[name].dtype)
    return out
```

```python
from contextlib import ExitStack

import concourse.bass as bass
from concourse import mybir

fp32 = mybir.dt.float32
u32 = mybir.dt.uint32
ALU = mybir.AluOpType
ACT = mybir.ActivationFunctionType
AX = mybir.AxisListType

P = 128
N, D, E = 12500, 32, 412500
RELS, BASES = 86, 16
J = 98
NP = P * J
K = 62
GROUPS = 52
T = K * GROUPS
EP = P * T
EB = 512
NEB = EP // EB
SB = 14
SH = SB // 2
PAIRS = GROUPS // 2
W0 = D + 2
RP = RELS // 2
HD = D // 2
W1 = D + 1 + HD
CN = 2 * D + RELS
JC = 2 * GROUPS
PB = 512 // D
BIG = 1.0e38
FAR = 4.0e6
SLOPE = 0.01
EPS = 1e-5
assert E <= EP and T * (P - 1) < E and N <= NP and EP % EB == 0 and J % SB == 0


class Order:

    def __init__(self, engine, sem):
        self.engine, self.sem, self.base, self.count, self.per = engine, sem, 0, 0, None

    def done(self, ins):
        ins.then_inc(self.sem, 1)
        self.count += 1
        self.engine.wait_ge(self.sem, self.base + self.count)

    def enter(self, iteration, per):
        self.start, self.per = self.count, per
        self.base, self.count = self.start + iteration * per, 0

    def leave(self, iterations):
        assert self.count == self.per, (self.count, self.per)
        self.base, self.count = 0, self.start + iterations * self.per


def build(nc, x, src, dst, etype, attn_w, weight, w_comp, self_w, a1_w, a1_b, a2_w, a2_b, rel_emb, out):
    def dram(name, shape, dt=fp32):
        return nc.dram_tensor(name, shape, dt, kind="Internal").ap()

    src_d = dram("src_padded", (EP, 1), u32)
    row_d = dram("row_of_edge", (EP, 1), u32)
    odd_d = dram("even_odd_relation", (EP, 2))
    dst_d = dram("dst_float", (EP, 1))
    last_d = dram("last_dst_of_block", (NEB,))
    end_d = dram("end_of_node", (1 + NP,))
    feat0_d = dram("layer0_rows", (NP, W0))
    sdst_d = dram("dst_scores", (NP, 1))
    z0_d = dram("dst_score_at_starts", (EP, 1))
    r0_d = dram("layer0_scans", (EP, W0))
    h1_d = dram("layer1_features", (NP, D))
    table_d = dram("layer1_rows", (NP * RP, 2 * W1))
    yhat_d = dram("y_hat", (NP, D))
    z1_d = dram("y_hat_at_starts", (EP, D))
    r1_d = dram("layer1_scans", (EP, D))

    with ExitStack() as ctx:
        def sb(name, shape, dt=fp32):
            return ctx.enter_context(nc.sbuf_tensor(name, shape, dt))

        def sem(name):
            return ctx.enter_context(nc.semaphore(name))

        cont = sb("same_dst_as_before", [P, T])
        sdst_e = sb("dst_score_of_edge", [P, JC * D])
        curr = sdst_e[:, :].rearrange("p (j c) -> p j c", c=D)
        xt = sb("x_nodes", [P, J, D])
        h = sb("h_nodes", [P, J, D + 1])
        agg = sb("aggregate_nodes", [P, J, W0])
        yhat = agg[:, :, :].rearrange("p j c -> p (j c)")[:, 0:J * D].rearrange("p (j c) -> p j c", c=D)
        zeros = sb("zeros", [P, T * D // K])
        wrel = sb("relation_weights", [D, RELS * D])
        wnode = sb("node_weights", [D + 1, CN])
        basis = sb("basis_weights", [BASES, D * D])
        comp_t = sb("w_comp_t", [BASES, RELS])
        rel_t = sb("rel_emb_t", [D, RELS])
        a1b = sb("a1_and_bias", [D, D + 1])
        wself = sb("self_loop_weights", [D, D])
        wattn = sb("attention_weights", [P, 2 * D])
        ident = sb("identity", [P, P])
        nid_u = sb("node_id_u", [P, J], u32)
        nid = sb("node_id", [P, J])
        kcnt = sb("block_of_node", [P, J])
        kblk = sb("block_index", [P, J], u32)
        ccnt = sb("count_in_block", [P, J])
        end = sb("end", [P, J])
        start = sb("start", [P, J])
        nonempty = sb("nonempty", [P, J])
        small = sb("small", [P, J])
        rstd = sb("rstd", [P, J])
        scat = sb("start_index", [P, J], u32)
        last = sb("last_edge_index", [P, J], u32)
        srclast = sb("src_of_last_edge", [P, J], u32)
        idx = sb("edge_row_index", [P, 2, K], u32)
        one = sb("chunk_scalars", [P, 16])
        first_u = sb("first_dst_index", [P, 1], u32)
        cedge_u = sb("first_segment_end_index", [P, 1], u32)
        cbase_u = sb("chunk_base_u", [P, 1], u32)
        prev, cnt, full, thr, cbase, cedge, y0init, mnew, mcar, e1, e2, cneg = (one[:, i:i + 1] for i in range(12))
        ylast = sb("last_y_hat", [P, D])
        odd = sb("even_odd", [P, 2, 2 * K])
        crow = sb("carry_row", [P, W0])
        cin = sb("carry_in", [P, 3, D + 1])
        cfix = sb("carry_fixed", [P, W0])
        cnb = sb("carry_back", [P, 2, D + 1])
        AW = 25800
        arena = sb("arena", [P, AW])

        def view(at, shape, dt=None):
            n = 1
            for s in shape:
                n *= s
            assert at + n <= AW
            v = arena[:, at:at + n]
            if dt is not None:
                v = v.bitcast(dt)
            if len(shape) == 2:
                v = v.rearrange("p (a b) -> p a b", b=shape[1])
            if len(shape) == 3:
                v = v.rearrange("p (a b c) -> p a b c", b=shape[1], c=shape[2])
            return v

        srci, eti, dsti, dstf = (view(i * T, [T], dt) for i, dt in enumerate((u32, u32, u32, None)))
        samples = view(4 * T, [NEB])
        junk = view(4 * T + NEB, [T])
        blocks = view(5 * T + NEB, [SB, EB])
        par = view(5 * T + NEB, [T, 2])
        rowi = eti
        z0 = view(0, [T])
        o = 0
        g0 = view(o, [2, K, W0]); o += 2 * K * W0
        r0 = view(o, [2, K, W0]); o += 2 * K * W0
        b0 = view(o, [K, D + 1]); o += K * (D + 1)
        e0 = view(o, [K]); o += K
        el0 = view(o, [K]); o += K
        neg0 = view(o, [K]); o += K
        tm0 = view(o, [K]); o += K
        m0 = view(o, [2, K + 1]); o += 2 * (K + 1)
        d0 = view(o, [2 * K]); o += 2 * K
        x0 = view(o, [2 * K]); o += 2 * K
        ct = view(o, [3 * P]); o += 3 * P
        cy = view(o, [P]); o += P
        cn = view(o, [P]); o += P
        cd = view(o, [2 * P]); o += 2 * P
        cf = view(o, [P]); o += P
        xc = view(0, [J, D])
        sq = view(J * D, [J, D])
        tb = view(0, [2, RP * 2, W1])
        o = 2 * RELS * W1
        hs = view(o, [2, D + 1]); o += 2 * (D + 1)
        hT = view(o, [2, P]); o += 2 * P
        xs = view(o, [2, D]); o += 2 * D
        o = 0
        g1 = view(o, [2, K, 2 * W1]); o += 2 * K * 2 * W1
        z1 = view(o, [2, K, D]); o += 2 * K * D
        m1 = view(o, [K, 2, D]); o += K * 2 * D
        r1 = view(o, [2, K, D]); o += 2 * K * D
        lg = view(o, [K]); o += K
        th = view(o, [K]); o += K
        av = view(o, [K]); o += K
        aw = view(o, [K, 2]); o += 2 * K
        pr = h[:, :, :].rearrange("p j c -> p (j c)")[:, 0:K * 2 * (HD + 1)].rearrange(
            "p (k a c) -> p k a c", a=2, c=HD + 1)
        ms = agg[:, :, :].rearrange("p j c -> p (j c)")[:, 0:K * D].rearrange("p (k c) -> p k c", c=D)
        cs = view(o, [2, D]); o += 2 * D
        cT = view(o, [2, P]); o += 2 * P
        ct1 = view(o, [2 * P]); o += 2 * P
        cn1 = view(o, [P]); o += P

        ps = ctx.enter_context(nc.psum_tensor("ps", [P, 8, 512], fp32))

        s_in = sem("s_in")
        s_x = sem("s_x")
        s_w = sem("s_w")
        s_pool_init = sem("s_pool_init")
        s_set = sem("s_set")
        s_v = sem("s_v")
        s_dstf = sem("s_dstf")
        s_dst_d = sem("s_dst_d")
        s_prev = sem("s_prev")
        s_last_d = sem("s_last_d")
        s_samples = sem("s_samples")
        s_row = sem("s_row")
        s_index_d = sem("s_index_d")
        s_kblk = sem("s_kblk")
        s_blk = [sem(f"s_blk{i}") for i in range(2)]
        s_blk_used = sem("s_blk_used")
        s_end = sem("s_end")
        s_end_d = sem("s_end_d")
        s_start = sem("s_start")
        s_nodeidx = sem("s_nodeidx")
        s_sqrt_in = sem("s_sqrt_in")
        s_sqrt = sem("s_sqrt")
        s_feat0 = sem("s_feat0")
        s_feat0_d = sem("s_feat0_d")
        s_zero_d = sem("s_zero_d")
        s_z0_d = sem("s_z0_d")
        s_z0 = sem("s_z0")
        s_y0init = sem("s_y0init")
        s_idx0 = [sem(f"s_idx0_{i}") for i in range(2)]
        s_g0 = [sem(f"s_g0_{i}") for i in range(2)]
        s_g0_free = sem("s_g0_free")
        s_d0 = sem("s_d0")
        s_x0 = sem("s_x0")
        s_r0 = sem("s_r0")
        s_r0_d = [sem(f"s_r0_d{i}") for i in range(2)]
        s_r0_free = sem("s_r0_free")
        s_srclast = sem("s_srclast")
        s_cin = sem("s_cin")
        s_ct = sem("s_ct")
        s_cd = sem("s_cd")
        s_cx = sem("s_cx")
        s_cback = sem("s_cback")
        s_cb = sem("s_cb")
        s_crow = sem("s_crow")
        s_ce = sem("s_ce")
        s_cex = sem("s_cex")
        s_cfix = sem("s_cfix")
        s_cfix_d = sem("s_cfix_d")
        s_agg0 = sem("s_agg0")
        s_h1 = sem("s_h1")
        s_h1_d = sem("s_h1_d")
        s_hl = sem("s_hl")
        s_wps = sem("s_wps")
        s_wrel = sem("s_wrel")
        s_hs = sem("s_hs")
        s_tp = sem("s_tp")
        s_hT = sem("s_hT")
        s_pnode = sem("s_pnode")
        s_pbank = sem("s_pbank")
        s_ev_act = sem("s_ev_act")
        s_ev_dve = sem("s_ev_dve")
        s_tb = [sem(f"s_tb{i}") for i in range(2)]
        s_tb_free = sem("s_tb_free")
        s_yhat_d = sem("s_yhat_d")
        s_z1_d = sem("s_z1_d")
        s_yinit = sem("s_yinit")
        s_idx1 = [sem(f"s_idx1_{i}") for i in range(2)]
        s_g1 = [sem(f"s_g1_{i}") for i in range(2)]
        s_g1_free = sem("s_g1_free")
        s_z1 = [sem(f"s_z1_{i}") for i in range(2)]
        s_ye = sem("s_ye")
        s_odd = [sem(f"s_odd{i}") for i in range(2)]
        s_lg = sem("s_lg")
        s_th = sem("s_th")
        s_r1 = sem("s_r1")
        s_r1_d = [sem(f"s_r1_d{i}") for i in range(2)]
        s_r1_free = sem("s_r1_free")
        s_cs = sem("s_cs")
        s_ctp = sem("s_ctp")
        s_cT = sem("s_cT")
        s_cmm = sem("s_cmm")
        s_curr = sem("s_curr")
        s_agg1 = sem("s_agg1")
        s_out = sem("s_out")
        s_out_d = sem("s_out_d")

        whole = P - 1
        cuts = [(0, 112), (112, 124), (124, 127)]
        e_rest, n_rest = E - whole * T, N - whole * J

        def edges(ap, lo, hi):
            return ap[lo * T:hi * T].rearrange("(p t) -> p t", t=T)

        def nodes(ap, lo, hi):
            return ap[lo * J:hi * J, :].rearrange("(p j) c -> p j c", j=J)

        def spread(ap, shape):
            return ap.unsqueeze(len(ap.shape)).to_broadcast(shape)

        block = ctx.enter_context(nc.Block())

        @block.sync
        def _(sp):
            sp.wait_ge(s_set, 1)
            for tile, ap in ((dsti, dst), (srci, src), (eti, etype)):
                ap = ap.bitcast(u32)
                for lo, hi in cuts:
                    sp.dma_start(tile[lo:hi, :], edges(ap, lo, hi)).then_inc(s_in, 16)
                sp.dma_start(tile[whole:P, 0:e_rest],
                             ap[whole * T:E].rearrange("(p t) -> p t", p=1)).then_inc(s_in, 16)
            for lo, hi in cuts:
                sp.dma_start(xt[lo:hi, :, :], nodes(x, lo, hi)).then_inc(s_x, 16)
            sp.dma_start(xt[whole:P, 0:n_rest, :],
                         x[whole * J:N, :].rearrange("(p j) c -> p j c", p=1)).then_inc(s_x, 16)
            sp.dma_start(wattn[:, :], attn_w.partition_broadcast(P)).then_inc(s_x, 16)
            sp.wait_ge(s_dstf, 1)
            dst_chunks = dst_d.rearrange("(p t) c -> p (t c)", t=T)
            sp.dma_start(dst_chunks, dstf).then_inc(s_dst_d, 16)
            sp.wait_ge(s_dst_d, 16)
            sp.dma_start(prev[1:P, :], dst_chunks[0:P - 1, T - 1:T],
                         allow_slow_non_contiguous=True).then_inc(s_prev, 16)
            sp.dma_start(last_d.rearrange("(k c) -> k c", c=1),
                         dst_d.rearrange("(k e) c -> k (e c)", e=EB)[:, EB - 1:EB],
                         allow_slow_non_contiguous=True).then_inc(s_last_d, 16)
            sp.wait_ge(s_last_d, 16)
            sp.dma_start(samples, last_d.partition_broadcast(P)).then_inc(s_samples, 16)
            sp.wait_ge(s_in, 12 * 16)
            sp.dma_start(src_d.rearrange("(p t) c -> p (t c)", t=T), srci).then_inc(s_index_d, 16)
            sp.wait_ge(s_row, 1)
            sp.dma_start(row_d.rearrange("(p t) c -> p (t c)", t=T), rowi).then_inc(s_index_d, 16)
            sp.dma_start(odd_d.rearrange("(p t) c -> p t c", t=T), par).then_inc(s_index_d, 16)
            sp.wait_ge(s_set, 2)
            half = T // 2
            for i in range(2):
                sp.dma_start(z0_d.rearrange("(p t) c -> p (t c)", t=T)[:, i * half:(i + 1) * half],
                             zeros[:, 0:half]).then_inc(s_zero_d, 16)
            sp.dma_start(end_d[0:1].rearrange("(a b) -> a b", a=1), zeros[0:1, 0:1]).then_inc(s_end_d, 16)
            sp.wait_ge(s_feat0, 1)
            f0 = feat0_d.rearrange("(p j) c -> p j c", j=J)
            sp.dma_start(f0, agg[:, :, :]).then_inc(s_feat0_d, 16)
            sp.dma_start(sdst_d.rearrange("(p j) c -> p (j c)", j=J), small[:, :]).then_inc(s_feat0_d, 16)
            sp.wait_ge(s_end, 1)
            sp.dma_start(end_d[1:1 + NP].rearrange("(p j) -> p j", j=J), end[:, :]).then_inc(s_end_d, 16)
            sp.wait_ge(s_end_d, 32)
            sp.dma_start(start[:, :], end_d[0:NP].rearrange("(p j) -> p j", j=J)).then_inc(s_start, 16)
            sp.dma_start(basis[:, :].rearrange("b (i o) -> b i o", o=D), weight).then_inc(s_w, 16)
            sp.dma_start(comp_t[:, :], w_comp.rearrange("r b -> b r"), allow_slow_non_contiguous=True).then_inc(s_w, 16)
            sp.dma_start(rel_t[:, :], rel_emb.rearrange("r a -> a r"), allow_slow_non_contiguous=True).then_inc(s_w, 16)
            sp.dma_start(a1b[:, 0:D], a1_w).then_inc(s_w, 16)
            sp.dma_start(a1b[:, D:D + 1], a1_b.rearrange("(a b) -> a b", b=1), allow_slow_non_contiguous=True).then_inc(s_w, 16)
            sp.dma_start(wself[:, :], self_w).then_inc(s_w, 16)
            sp.dma_start(wnode[0:D, 0:D], a1_w.rearrange("o i -> i o"), allow_slow_non_contiguous=True).then_inc(s_w, 16)
            sp.dma_start(wnode[0:D, D:2 * D], a2_w.rearrange("o i -> i o"), allow_slow_non_contiguous=True).then_inc(s_w, 16)
            sp.dma_start(wnode[D:D + 1, 0:D], a1_b.rearrange("(a b) -> a b", a=1)).then_inc(s_w, 16)
            sp.dma_start(wnode[D:D + 1, D:2 * D], a2_b.rearrange("(a b) -> a b", a=1)).then_inc(s_w, 16)
            sp.wait_ge(s_index_d, 48)
            src_c = src_d.rearrange("(p t) c -> p (t c)", t=T)
            row_c = row_d.rearrange("(p t) c -> p (t c)", t=T)
            for b in range(2):
                sp.dma_start(idx[:, b, :], src_c[:, b * K:(b + 1) * K]).then_inc(s_idx0[b], 16)
            sp.wait_ge(s_z0_d, 16 * J)
            sp.dma_start(z0, z0_d.rearrange("(p t) c -> p (t c)", t=T)).then_inc(s_z0, 16)
            sp.dma_start(z1_d.rearrange("(p k t) c -> p k (t c)", p=P, k=K),
                         zeros[:, :].unsqueeze(1).to_broadcast([P, K, T * D // K])).then_inc(s_zero_d, 16)

            r0_c = r0_d.rearrange("(p t) c -> p t c", t=T)

            def store0(b, g, turn):
                sp.wait_ge(s_r0, g + 1)
                sp.dma_start(r0_c[:, bass.ds(g * K, K), :], r0[:, b, :, :]).then_inc(s_r0_d[b], 16)
                sp.wait_ge(s_r0_d[b], 16 * turn)
                sp.sem_inc(s_r0_free, 1)

            with sp.Fori(0, PAIRS - 1) as it:
                for b in range(2):
                    sp.wait_ge(s_g0[b], 16 * K * (it + 1))
                    sp.dma_start(idx[:, b, :], src_c[:, bass.ds((2 * it + b + 2) * K, K)]).then_inc(s_idx0[b], 16)
                    store0(b, 2 * it + b, it + 1)
            for b in range(2):
                store0(b, GROUPS - 2 + b, PAIRS)

            sp.wait_ge(s_h1, 1)
            sp.dma_start(h1_d.rearrange("(p j) c -> p j c", j=J), h[:, :, 0:D]).then_inc(s_h1_d, 16)
            for b in range(2):
                sp.wait_ge(s_g0[b], 16 * K * PAIRS)
                sp.dma_start(idx[:, b, :], row_c[:, b * K:(b + 1) * K]).then_inc(s_idx1[b], 16)
            t_j = table_d.rearrange("(p j r) c -> p j (r c)", j=J, r=RP)

            def store_table(b, n):
                sp.wait_ge(s_ev_act, 6 * n + 12)
                sp.wait_ge(s_ev_dve, 4 * n + 8)
                sp.dma_start(t_j[:, bass.ds(n, 1), :].rearrange("p a c -> p (a c)"),
                             tb[:, b, :, :].rearrange("p r c -> p (r c)")).then_inc(s_tb[b], 16)

            store_table(0, 0)
            with sp.Fori(0, J // 2 - 1) as it:
                for b in (1, 0):
                    store_table(b, 2 * it + 2 - b)
                    sp.wait_ge(s_tb[1 - b], 16 * (it + 1))
                    sp.sem_inc(s_tb_free, 1)
            store_table(1, J - 1)
            sp.dma_start(yhat_d.rearrange("(p j) c -> p j c", j=J), yhat).then_inc(s_yhat_d, 16)
            for b in range(2):
                sp.wait_ge(s_tb[b], 16 * J // 2)
            sp.sem_inc(s_tb_free, 2)
            sp.wait_ge(s_z1_d, 16 * J)
            z1_c = z1_d.rearrange("(p t) c -> p t c", t=T)
            odd_c = odd_d.rearrange("(p t) c -> p (t c)", t=T)
            r1_c = r1_d.rearrange("(p t) c -> p t c", t=T)

            def load1(b, at):
                sp.dma_start(z1[:, b, :, :], z1_c[:, bass.ds(at, K), :]).then_inc(s_z1[b], 16)

            def load_odd(b, at):
                sp.dma_start(odd[:, b, :], odd_c[:, bass.ds(at * 2, 2 * K)]).then_inc(s_odd[b], 16)

            def store1(b, g, turn):
                sp.wait_ge(s_r1, g + 1)
                sp.dma_start(r1_c[:, bass.ds(g * K, K), :], r1[:, b, :, :]).then_inc(s_r1_d[b], 16)
                sp.wait_ge(s_r1_d[b], 16 * turn)
                sp.sem_inc(s_r1_free, 1)

            for b in range(2):
                load1(b, b * K)
                load_odd(b, b * K)
            with sp.Fori(0, PAIRS - 1) as it:
                for b in range(2):
                    sp.wait_ge(s_g1[b], 16 * K * (it + 1))
                    sp.dma_start(idx[:, b, :], row_c[:, bass.ds((2 * it + b + 2) * K, K)]).then_inc(s_idx1[b], 16)
                    sp.wait_ge(s_lg, 2 * it + b + 1)
                    load1(b, (2 * it + b + 2) * K)
                    store1(b, 2 * it + b, it + 1)
                    load_odd(b, (2 * it + b + 2) * K)
            for b in range(2):
                store1(b, GROUPS - 2 + b, PAIRS)
            sp.wait_ge(s_out, 1)
            for lo, hi in cuts:
                sp.dma_start(nodes(out, lo, hi), xt[lo:hi, :, :]).then_inc(s_out_d, 16)
            sp.dma_start(out[whole * J:N, :].rearrange("(p j) c -> p j c", p=1),
                         xt[whole:P, 0:n_rest, :]).then_inc(s_out_d, 16)
            sp.wait_ge(s_out_d, 4 * 16)
            sp.wait_ge(s_zero_d, 3 * 16)
            sp.wait_ge(s_feat0_d, 2 * 16)
            sp.wait_ge(s_h1_d, 16)
            sp.wait_ge(s_yhat_d, 16)
            sp.wait_ge(s_cfix_d, 32)

        @block.gpsimd
        def _(pool):
            def gather(tile, table, index, done):
                pool.indirect_dma_start(tile, None, table, bass.IndirectOffsetOnAxis(ap=index, axis=0)) \
                    .then_inc(done, 16)

            pool.iota(nid_u[:, :], [[1, J]], base=0, channel_multiplier=J).then_inc(s_pool_init, 1)
            pool.iota(cbase_u[:, :], [[0, 1]], base=0, channel_multiplier=T).then_inc(s_pool_init, 1)
            pool.memset(ident[:, :], 0.0).then_inc(s_pool_init, 1)
            pool.wait_ge(s_pool_init, 3)
            pool.affine_select(out=ident[:, :], in_=ident[:, :], compare_op=ALU.not_equal, fill=1.0,
                               base=0, pattern=[[-1, P]], channel_multiplier=1).then_inc(s_pool_init, 1)
            pool.wait_ge(s_kblk, 1)
            pool.wait_ge(s_dst_d, 16)
            pool.wait_ge(s_index_d, 48)
            dst_b = dst_d.rearrange("(k e) c -> k (e c)", e=EB)
            for j in range(J):
                if j % SH == 0 and j >= SB:
                    pool.wait_ge(s_blk_used, j // SH - 1)
                gather(blocks[:, j % SB, :], dst_b, kblk[:, j:j + 1], s_blk[j // SH % 2])
            pool.wait_ge(s_nodeidx, 1)
            pool.wait_ge(s_zero_d, 32)
            pool.wait_ge(s_feat0_d, 32)
            gather(y0init, sdst_d, first_u[:, 0:1], s_y0init)
            for j in range(J):
                pool.indirect_dma_start(z0_d, bass.IndirectOffsetOnAxis(ap=scat[:, j:j + 1], axis=0),
                                        small[:, j:j + 1], None, bounds_check=EP - 1, oob_is_err=False) \
                    .then_inc(s_z0_d, 16)
            pool.wait_ge(s_z0, 16)
            with pool.Fori(0, PAIRS) as it:
                for b in range(2):
                    pool.wait_ge(s_idx0[b], 16 * (it + 1))
                    pool.wait_ge(s_g0_free, 2 * it + b + 1)
                    pool.nop(nofuse=True)
                    for k in range(K):
                        gather(g0[:, b, k, :], feat0_d, idx[:, b, k:k + 1], s_g0[b])
            for j in range(J):
                gather(srclast[:, j:j + 1], src_d, last[:, j:j + 1], s_srclast)

            def fix(rows, width, all_stored, turn):
                pool.wait_ge(all_stored, GROUPS + 2)
                gather(crow[:, 0:width], rows, cedge_u[:, 0:1], s_crow)
                pool.wait_ge(s_cfix, turn)
                pool.indirect_dma_start(rows, bass.IndirectOffsetOnAxis(ap=cedge_u[:, 0:1], axis=0),
                                        cfix[:, 0:width], None).then_inc(s_cfix_d, 16)
                pool.wait_ge(s_cfix_d, 16 * turn)

            fix(r0_d, W0, s_r0_free, 1)
            for j in range(J):
                gather(agg[:, j, :], r0_d, last[:, j:j + 1], s_agg0)
            pool.wait_ge(s_h1_d, 16)
            pool.wait_ge(s_srclast, 16 * J)
            for j in range(J):
                gather(curr[:, j, :], h1_d, srclast[:, j:j + 1], s_hl)
            pool.wait_ge(s_zero_d, 48)
            for j in range(J):
                pool.wait_ge(s_ev_act, 6 * j + 12)
                pool.indirect_dma_start(z1_d, bass.IndirectOffsetOnAxis(ap=scat[:, j:j + 1], axis=0),
                                        yhat[:, j, :], None, bounds_check=EP - 1, oob_is_err=False) \
                    .then_inc(s_z1_d, 16)
            pool.wait_ge(s_yhat_d, 16)
            gather(ylast[:, :], yhat_d, first_u[:, 0:1], s_yinit)
            pool.wait_ge(s_tb_free, J + 2)
            with pool.Fori(0, PAIRS) as it:
                for b in range(2):
                    pool.wait_ge(s_idx1[b], 16 * (it + 1))
                    pool.wait_ge(s_g1_free, 2 * it + b + 1)
                    pool.nop(nofuse=True)
                    for k in range(K):
                        gather(g1[:, b, k, :], table_d, idx[:, b, k:k + 1], s_g1[b])
            fix(r1_d, D, s_r1_free, 2)
            for j in range(J):
                gather(yhat[:, j, :], r1_d, last[:, j:j + 1], s_agg1)

        @block.scalar
        def _(act):
            act.wait_ge(s_sqrt_in, 1)
            act.activation(rstd[:, :], small[:, :], ACT.Sqrt).then_inc(s_sqrt, 1)
            act.wait_ge(s_wps, 1)
            per = 5
            for q in range(0, D, per):
                n = min(per, D - q)
                act.activation(wrel[:, :].rearrange("i (r o) -> i o r", o=D)[:, q:q + n, :],
                               ps[0:D, q // per, 0:n * RELS].rearrange("i (o r) -> i o r", r=RELS),
                               ACT.Copy).then_inc(s_wrel, 1)
            act.activation(wnode[:, 2 * D:CN], ps[0:D + 1, 7, 0:RELS], ACT.Copy).then_inc(s_wrel, 1)
            with act.Fori(0, GROUPS) as g:
                act.wait_ge(s_d0, g + 1)
                act.activation(x0, d0, ACT.Exp).then_inc(s_x0, 1)
            act.wait_ge(s_cd, 1)
            act.activation(cd[0:D + 1, :], cd[0:D + 1, :], ACT.Exp).then_inc(s_cx, 1)
            act.wait_ge(s_ce, 1)
            act.activation(one[:, 9:11], one[:, 9:11], ACT.Exp).then_inc(s_cex, 1)
            act.wait_ge(s_sqrt_in, 2)
            act.activation(rstd[:, :], small[:, :], ACT.Sqrt).then_inc(s_sqrt, 1)
            act.wait_ge(s_h1, 1)
            act.sem_inc(s_ev_act, 6)
            with act.Fori(0, J // 2) as it:
                for b in range(2):
                    n = 2 * it + b
                    act.wait_ge(s_tp, n + 1)
                    act.nop(nofuse=True)
                    act.activation(hs[:, b, :], h[:, bass.ds(n, 1), :].rearrange("p a c -> p (a c)"),
                                   ACT.Copy).then_inc(s_hs, 1)
                    act.wait_ge(s_tp, n + 2)
                    act.activation(hT[0:D + 1, b, :], ps[0:D + 1, 7, 0:P], ACT.Copy).then_inc(s_hT, 1)
                    act.wait_ge(s_tb_free, n + 1)
                    for q in (0, 2, 4):
                        act.wait_ge(s_pbank, 6 * n + q + 1)
                        act.activation(tb[:, b, q * PB:(q + 1) * PB, 0:D],
                                       ps[:, q, :].rearrange("p (r c) -> p r c", c=D),
                                       ACT.Copy).then_inc(s_ev_act, 1)
                    act.wait_ge(s_pnode, n + 1)
                    act.activation(xs[:, b, :], ps[:, 6, 0:D], ACT.Copy).then_inc(s_ev_act, 1)
                    act.activation(tb[:, b, :, D], ps[:, 6, 2 * D:CN], ACT.Copy).then_inc(s_ev_act, 1)
                    act.activation(yhat[:, bass.ds(n, 1), :].rearrange("p a c -> p (a c)"), ps[:, 6, D:2 * D],
                                   ACT.Copy).then_inc(s_ev_act, 1)
            act.wait_ge(s_hl, 16 * J)
            with act.Fori(0, GROUPS) as g:
                act.wait_ge(s_lg, g + 1)
                act.activation(th, lg, ACT.Tanh, scale=float(D) ** -0.5).then_inc(s_th, 1)
                for i in range(2):
                    act.activation(cs[:, i, :], curr[:, bass.ds(2 * g + i, 1), :].rearrange("p a c -> p (a c)"),
                                   ACT.Copy).then_inc(s_cs, 1)
                act.wait_ge(s_ctp, g + 1)
                act.activation(cT[0:D, :, :].rearrange("c i p -> c (i p)"), ps[0:D, 4, 0:2 * P],
                               ACT.Copy).then_inc(s_cT, 1)
                act.wait_ge(s_cmm, g + 1)
                act.nop(nofuse=True)
                act.activation(curr[:, bass.ds(2 * g, 2), :].rearrange("p a c -> p (a c)"), ps[:, 5, 0:2 * D],
                               ACT.Copy).then_inc(s_curr, 1)

        @block.tensor
        def _(pe):
            pe.wait_ge(s_w, 160)
            bas = basis[:, :].rearrange("b (i o) -> b i o", o=D)
            for q in range(D):
                nc.tensor.matmul(ps[0:D, q // 5, q % 5 * RELS:(q % 5 + 1) * RELS], bas[:, :, q], comp_t[:, :],
                                 start=True, stop=True)
            nc.tensor.matmul(ps[0:D + 1, 7, 0:RELS], a1b[:, :], rel_t[:, :], start=True, stop=True) \
                .then_inc(s_wps, 1)
            pe.wait_ge(s_pool_init, 4)

            pe.wait_ge(s_wrel, 8)
            pe.wait_ge(s_cin, 1)
            for i in range(3):
                ins = nc.tensor.transpose(ps[0:D + 1, 0, i * P:(i + 1) * P], cin[:, i, :], ident[:, :])
            ins.then_inc(s_ct, 1)
            pe.wait_ge(s_cback, 1)
            nc.tensor.transpose(ps[:, 1, 0:D + 1], cn[0:D + 1, :], ident[0:D + 1, 0:D + 1])
            nc.tensor.transpose(ps[:, 1, D + 1:2 * D + 2], cy[0:D + 1, :], ident[0:D + 1, 0:D + 1]) \
                .then_inc(s_cb, 1)
            pe.wait_ge(s_h1, 1)
            pe.nop(nofuse=True).then_inc(s_tp, 1)
            with pe.Fori(0, J // 2) as it:
                for b in range(2):
                    n = 2 * it + b
                    pe.wait_ge(s_hs, n + 1)
                    pe.nop(nofuse=True)
                    nc.tensor.transpose(ps[0:D + 1, 7, 0:P], hs[:, b, :], ident[:, :]).then_inc(s_tp, 1)
                    pe.wait_ge(s_hT, n + 1)
                    for q in range(6):
                        if q % 2 == 0:
                            pe.wait_ge(s_ev_act, 6 * n + q // 2 + 1)
                        else:
                            pe.wait_ge(s_ev_dve, 4 * n + q // 2 + 1)
                        cols = min(PB, RELS - q * PB) * D
                        nc.tensor.matmul(ps[:, q, 0:cols], hT[0:D, b, :], wrel[:, q * 512:q * 512 + cols],
                                         start=True, stop=True).then_inc(s_pbank, 1)
                    pe.wait_ge(s_ev_act, 6 * n + 6)
                    nc.tensor.matmul(ps[:, 6, 0:CN], hT[0:D + 1, b, :], wnode[:, :], start=True, stop=True) \
                        .then_inc(s_pnode, 1)
            with pe.Fori(0, GROUPS) as g:
                pe.wait_ge(s_cs, 2 * g + 2)
                for i in range(2):
                    ins = nc.tensor.transpose(ps[0:D, 4, i * P:(i + 1) * P], cs[:, i, :], ident[:, :])
                ins.then_inc(s_ctp, 1)
                pe.wait_ge(s_cT, g + 1)
                for i in range(2):
                    ins = nc.tensor.matmul(ps[:, 5, i * D:(i + 1) * D], cT[0:D, i, :], wself[:, :],
                                           start=True, stop=True)
                ins.then_inc(s_cmm, 1)
            pe.wait_ge(s_cin, 2)
            for i in range(2):
                ins = nc.tensor.transpose(ps[0:D, 0, i * P:(i + 1) * P], cin[:, i, 0:D], ident[:, :])
            ins.then_inc(s_ct, 1)
            pe.wait_ge(s_cback, 2)
            nc.tensor.transpose(ps[:, 1, 0:D], cn1[0:D, :], ident[0:D, 0:D]).then_inc(s_cb, 1)

        @block.vector
        def _(v):
            order = Order(v, s_v)
            done = order.done

            pad = e_rest
            v.memset(srci[:, pad:T], 0)
            v.memset(eti[:, pad:T], 0)
            v.memset(prev, -1.0)
            v.memset(xt[:, :, :], 0.0)
            v.memset(dsti[:, pad:T], NP - 1).then_inc(s_set, 1)
            v.memset(zeros[:, :], 0.0).then_inc(s_set, 1)
            v.memset(h[:, :, D:D + 1], 1.0)
            v.wait_ge(s_pool_init, 2)
            v.tensor_copy(nid[:, :], nid_u[:, :])
            done(v.tensor_copy(cbase, cbase_u[:, :]))

            v.wait_ge(s_in, 12 * 16)
            v.tensor_copy(dstf, dsti).then_inc(s_dstf, 1)
            v.tensor_copy(first_u[:, :], dsti[:, 0:1])
            v.wait_ge(s_dstf, 1)
            hrow = junk.bitcast(u32)
            done(v.tensor_scalar(hrow, eti, 1, None, ALU.logical_shift_right))
            done(v.scalar_tensor_tensor(out=par[:, :, 1], in0=hrow, scalar=-2.0, in1=eti, op0=ALU.mult, op1=ALU.add))
            done(v.scalar_tensor_tensor(out=rowi, in0=srci, scalar=float(RP), in1=hrow, op0=ALU.mult, op1=ALU.add))
            v.tensor_scalar(par[:, :, 0], par[:, :, 1], -1.0, 1.0, ALU.mult, ALU.add).then_inc(s_row, 1)
            v.tensor_tensor(cont[:, 1:T], dstf[:, 1:T], dstf[:, 0:T - 1], ALU.is_equal)
            done(v.tensor_scalar(junk, dstf, dstf[:, 0:1], None, ALU.is_equal, ALU.add, accum_out=cnt))
            v.wait_ge(s_prev, 16)
            done(v.tensor_tensor(cont[:, 0:1], dstf[:, 0:1], prev, ALU.is_equal))
            v.tensor_scalar(full, cnt, float(T), None, ALU.is_equal)
            done(v.tensor_tensor(cedge, cbase, cnt, ALU.add))
            v.tensor_tensor(thr, full, cont[:, 0:1], ALU.mult)
            done(v.tensor_scalar(cedge_u[:, :], cedge, -1.0, None, ALU.add))

            v.wait_ge(s_samples, 16)
            for j in range(J):
                done(v.tensor_scalar(junk[:, 0:NEB], samples, nid[:, j:j + 1], None, ALU.is_le, ALU.add,
                                     accum_out=kcnt[:, j:j + 1]))
            done(v.tensor_scalar(kcnt[:, :], kcnt[:, :], float(NEB - 1), None, ALU.min))
            v.tensor_copy(kblk[:, :], kcnt[:, :]).then_inc(s_kblk, 1)

            def layer_norm(turn, xc, sq):
                done(v.tensor_reduce(small[:, :], xt[:, :, :], AX.X, ALU.add))
                done(v.tensor_scalar(small[:, :], small[:, :], -1.0 / D, None, ALU.mult))
                done(v.tensor_tensor(xc, xt[:, :, :], spread(small[:, :], [P, J, D]), ALU.add))
                done(v.tensor_tensor(sq, xc, xc, ALU.mult))
                done(v.tensor_reduce(small[:, :], sq, AX.X, ALU.add))
                v.tensor_scalar(small[:, :], small[:, :], 1.0 / D, EPS, ALU.mult, ALU.add).then_inc(s_sqrt_in, 1)
                v.wait_ge(s_sqrt, turn)
                done(v.reciprocal(small[:, :], rstd[:, :]))
                done(v.tensor_tensor(sq, xc, spread(small[:, :], [P, J, D]), ALU.mult))
                return v.tensor_scalar(h[:, :, 0:D], sq, 0.0, None, ALU.max)

            v.wait_ge(s_x, 5 * 16)
            xc0 = agg[:, :, 0:D]
            sq0 = curr[:, 0:J, :]
            done(layer_norm(1, xc0, sq0))
            for half in range(2):
                w = wattn[:, half * D:(half + 1) * D].unsqueeze(1).to_broadcast([P, J, D])
                done(v.tensor_tensor(sq0, h[:, :, 0:D], w, ALU.mult))
                to = agg[:, :, D + 1] if half == 0 else small[:, :]
                done(v.tensor_reduce(to, sq0, AX.X, ALU.add))
            v.tensor_copy(agg[:, :, 0:D + 1], h[:, :, :]).then_inc(s_feat0, 1)

            for q in range(J // SH):
                v.wait_ge(s_blk[q % 2], 16 * SH * (q // 2 + 1))
                for i in range(SH):
                    j = q * SH + i
                    ins = v.tensor_scalar(junk[:, 0:EB], blocks[:, j % SB, :], nid[:, j:j + 1], None, ALU.is_le,
                                          ALU.add, accum_out=ccnt[:, j:j + 1])
                    if i < SH - 1:
                        done(ins)
                ins.then_inc(s_blk_used, 1)
                v.wait_ge(s_blk_used, q + 1)
            v.scalar_tensor_tensor(out=end[:, :], in0=kcnt[:, :], scalar=float(EB), in1=ccnt[:, :], op0=ALU.mult,
                                   op1=ALU.add).then_inc(s_end, 1)
            v.wait_ge(s_start, 16)
            done(v.tensor_tensor(nonempty[:, :], start[:, :], end[:, :], ALU.is_lt))
            done(v.tensor_scalar(kcnt[:, :], nonempty[:, :], -FAR, FAR, ALU.mult, ALU.add))
            v.tensor_tensor(scat[:, :], start[:, :], kcnt[:, :], ALU.add)
            v.tensor_scalar(last[:, :], end[:, :], -1.0, 0.0, ALU.add, ALU.max).then_inc(s_nodeidx, 1)

            v.wait_ge(s_z0, 16)
            v.wait_ge(s_y0init, 16)
            v.wait_ge(s_nodeidx, 1)
            done(v.tensor_tensor_scan(sdst_e[:, 0:T], cont[:, :], z0, y0init, ALU.mult, ALU.add))

            v.memset(m0[:, 1, K:K + 1], -BIG).then_inc(s_g0_free, 2)
            v.memset(r0[:, 1, K - 1:K, :], 0.0).then_inc(s_r0_free, 2)
            v.wait_ge(s_r0_free, 2)
            with v.Fori(0, PAIRS) as it:
                order.enter(it, 10)
                for b in range(2):
                    g = 2 * it + b
                    at = bass.ds(g * K, K)
                    v.wait_ge(s_g0[b], 16 * K * (it + 1))
                    v.tensor_scalar(neg0, cont[:, at], BIG, -BIG, ALU.mult, ALU.add)
                    done(v.tensor_tensor(e0, g0[:, b, :, D + 1], sdst_e[:, at], ALU.add))
                    done(v.scalar_tensor_tensor(out=el0, in0=e0, scalar=SLOPE, in1=e0, op0=ALU.mult, op1=ALU.max))
                    v.tensor_copy(m0[:, b, 0:1], m0[:, 1 - b, K:K + 1])
                    done(v.tensor_tensor_scan(m0[:, b, 1:K + 1], neg0, el0, m0[:, 1 - b, K:K + 1], ALU.add, ALU.max))
                    v.tensor_tensor(d0[:, K:2 * K], el0, m0[:, b, 1:K + 1], ALU.subtract)
                    done(v.tensor_tensor(tm0, m0[:, b, 0:K], neg0, ALU.add))
                    v.tensor_tensor(d0[:, 0:K], tm0, m0[:, b, 1:K + 1], ALU.subtract).then_inc(s_d0, 1)
                    v.wait_ge(s_x0, g + 1)
                    v.tensor_tensor(b0, g0[:, b, :, 0:D + 1], spread(x0[:, K:2 * K], [P, K, D + 1]), ALU.mult) \
                        .then_inc(s_g0_free, 1)
                    v.wait_ge(s_g0_free, g + 3)
                    v.wait_ge(s_r0_free, g + 1)
                    done(v.tensor_copy(r0[:, b, :, D + 1], m0[:, b, 1:K + 1]))
                    for c in range(D + 1):
                        ins = v.tensor_tensor_scan(r0[:, b, :, c], x0[:, 0:K], b0[:, :, c],
                                                   r0[:, 1 - b, K - 1, c:c + 1], ALU.mult, ALU.add)
                    ins.then_inc(s_r0, 1)
                    v.wait_ge(s_r0, g + 1)
                order.leave(PAIRS)

            F, C = D + 1, P - 1
            tail = r0[:, 1, K - 1, :]
            v.tensor_copy(cin[:, 0, :], tail[:, 0:F])
            v.tensor_copy(cin[:, 1, :], tail[:, F:F + 1].to_broadcast([P, F]))
            v.tensor_scalar(cin[:, 2, :], thr.to_broadcast([P, F]), BIG, -BIG, ALU.mult, ALU.add).then_inc(s_cin, 1)
            v.tensor_scalar(cneg, cont[:, 0:1], BIG, -BIG, ALU.mult, ALU.add)
            v.memset(cd[0:F, :], 0.0)
            v.memset(cy[0:F, 0:1], -BIG)
            v.memset(cn[0:F, 0:1], 0.0)
            v.wait_ge(s_ct, 1)
            done(v.tensor_copy(ct[0:F, :], ps[0:F, 0, 0:3 * P]))
            sums, maxs, negs = (ct[0:F, i * P:i * P + C] for i in range(3))
            done(v.tensor_tensor_scan(cy[0:F, 1:P], negs, maxs, -BIG, ALU.add, ALU.max))
            done(v.tensor_tensor(cf[0:F, 0:C], cy[0:F, 0:C], negs, ALU.add))
            v.tensor_tensor(cd[0:F, 0:C], cf[0:F, 0:C], cy[0:F, 1:P], ALU.subtract)
            v.tensor_tensor(cd[0:F, P:P + C], maxs, cy[0:F, 1:P], ALU.subtract).then_inc(s_cd, 1)
            v.wait_ge(s_cx, 1)
            done(v.tensor_tensor(cf[0:F, 0:C], sums, cd[0:F, P:P + C], ALU.mult))
            v.tensor_tensor_scan(cn[0:F, 1:P], cd[0:F, 0:C], cf[0:F, 0:C], 0.0, ALU.mult, ALU.add) \
                .then_inc(s_cback, 1)
            v.wait_ge(s_cb, 1)
            done(v.tensor_copy(cnb[:, :, :], ps[:, 1, 0:2 * F].rearrange("p (a b) -> p a b", b=F)))
            done(v.tensor_tensor(mcar, cnb[:, 1, 0:1], cneg, ALU.add))
            v.wait_ge(s_crow, 16)
            done(v.tensor_tensor(mnew, crow[:, F:F + 1], mcar, ALU.max))
            v.tensor_tensor(e1, crow[:, F:F + 1], mnew, ALU.subtract)
            v.tensor_tensor(e2, mcar, mnew, ALU.subtract).then_inc(s_ce, 1)
            v.wait_ge(s_cex, 1)
            done(v.tensor_scalar(crow[:, 0:F], crow[:, 0:F], e1, None, ALU.mult))
            v.tensor_copy(cfix[:, F:F + 1], mnew)
            v.scalar_tensor_tensor(out=cfix[:, 0:F], in0=cnb[:, 0, :], scalar=e2, in1=crow[:, 0:F], op0=ALU.mult,
                                   op1=ALU.add).then_inc(s_cfix, 1)

            v.memset(curr[:, J:JC, :], 0.0)
            v.wait_ge(s_agg0, 16 * J)
            done(v.reciprocal(small[:, :], agg[:, :, D]))
            done(v.tensor_tensor(small[:, :], small[:, :], nonempty[:, :], ALU.mult))
            done(v.tensor_tensor(sq, agg[:, :, 0:D], spread(small[:, :], [P, J, D]), ALU.mult))
            done(v.tensor_tensor(xt[:, :, :], xt[:, :, :], sq, ALU.add))
            layer_norm(2, xc, sq).then_inc(s_h1, 1)

            v.wait_ge(s_h1, 1)
            v.memset(small[:, 0:1], 0.0).then_inc(s_tb_free, 2)
            v.memset(small[:, 1:2], 0.0).then_inc(s_ev_dve, 4)
            with v.Fori(0, J // 2) as it:
                for b in range(2):
                    n = 2 * it + b
                    v.wait_ge(s_tb_free, n + 1)
                    for q in (1, 3, 5):
                        rels = min(PB, RELS - q * PB)
                        v.wait_ge(s_pbank, 6 * n + q + 1)
                        v.tensor_copy(tb[:, b, q * PB:q * PB + rels, 0:D],
                                      ps[:, q, 0:rels * D].rearrange("p (r c) -> p r c", c=D)).then_inc(s_ev_dve, 1)
                    v.wait_ge(s_ev_act, 6 * n + 10)
                    v.tensor_copy(tb[:, b, :, D + 1:W1].rearrange("p (r a) c -> p r a c", a=2),
                                  xs[:, b, :].rearrange("p (a c) -> p a c", a=2).unsqueeze(1)
                                  .to_broadcast([P, RP, 2, HD])).then_inc(s_ev_dve, 1)

            v.wait_ge(s_yinit, 16)
            v.memset(av, 0.0).then_inc(s_g1_free, 2)
            v.memset(r1[:, 1, K - 1:K, :], 0.0).then_inc(s_r1_free, 2)
            v.wait_ge(s_r1_free, 2)
            v.wait_ge(s_g1_free, 2)
            with v.Fori(0, PAIRS) as it:
                order.enter(it, 10)
                for b in range(2):
                    g = 2 * it + b
                    at = bass.ds(g * K, K)
                    v.wait_ge(s_z1[b], 16 * (it + 1))
                    for c in range(D):
                        ins = v.tensor_tensor_scan(z1[:, b, :, c], cont[:, at], z1[:, b, :, c], ylast[:, c:c + 1],
                                                   ALU.mult, ALU.add)
                    done(ins)
                    v.tensor_copy(ylast[:, :], z1[:, b, K - 1, :])
                    v.wait_ge(s_g1[b], 16 * K * (it + 1))
                    v.wait_ge(s_odd[b], 16 * (it + 1))
                    rows = g1[:, b, :, :].rearrange("p k (a c) -> p k a c", a=2)
                    which = odd[:, b, :].rearrange("p (k a) -> p k a", a=2)
                    v.tensor_tensor(pr[:, :, :, HD], rows[:, :, :, D], which, ALU.mult)
                    done(v.tensor_tensor(pr[:, :, :, 0:HD], rows[:, :, :, D + 1:W1],
                                         z1[:, b, :, :].rearrange("p k (a c) -> p k a c", a=2), ALU.mult))
                    v.tensor_reduce(lg, pr.rearrange("p k a c -> p k (a c)"), AX.X, ALU.add).then_inc(s_lg, 1)
                    v.wait_ge(s_th, g + 1)
                    done(v.tensor_scalar(av, th, 0.0, None, ALU.max))
                    done(v.tensor_tensor(aw, which, spread(av, [P, K, 2]), ALU.mult))
                    v.tensor_tensor(m1, rows[:, :, :, 0:D], spread(aw, [P, K, 2, D]), ALU.mult) \
                        .then_inc(s_g1_free, 1)
                    v.wait_ge(s_g1_free, g + 3)
                    done(v.tensor_tensor(ms, m1[:, :, 0, :], m1[:, :, 1, :], ALU.add))
                    v.wait_ge(s_r1_free, g + 1)
                    for c in range(D):
                        ins = v.tensor_tensor_scan(r1[:, b, :, c], cont[:, at], ms[:, :, c],
                                                   r1[:, 1 - b, K - 1, c:c + 1], ALU.mult, ALU.add)
                    ins.then_inc(s_r1, 1)
                    v.wait_ge(s_r1, g + 1)
                order.leave(PAIRS)

            v.tensor_copy(cin[:, 0, 0:D], r1[:, 1, K - 1, :])
            v.tensor_copy(cin[:, 1, 0:D], thr.to_broadcast([P, D])).then_inc(s_cin, 1)
            v.memset(cn1[0:D, 0:1], 0.0)
            v.wait_ge(s_ct, 2)
            done(v.tensor_copy(ct1[0:D, :], ps[0:D, 0, 0:2 * P]))
            v.tensor_tensor_scan(cn1[0:D, 1:P], ct1[0:D, P:P + C], ct1[0:D, 0:C], 0.0, ALU.mult, ALU.add) \
                .then_inc(s_cback, 1)
            v.wait_ge(s_cb, 2)
            done(v.tensor_copy(cnb[:, 0, 0:D], ps[:, 1, 0:D]))
            v.wait_ge(s_crow, 32)
            v.scalar_tensor_tensor(out=cfix[:, 0:D], in0=cnb[:, 0, 0:D], scalar=cont[:, 0:1], in1=crow[:, 0:D],
                                   op0=ALU.mult, op1=ALU.add).then_inc(s_cfix, 1)
            v.wait_ge(s_agg1, 16 * J)
            v.wait_ge(s_curr, GROUPS)
            done(v.tensor_tensor(yhat, yhat, curr[:, 0:J, :], ALU.add))
            done(v.tensor_tensor(yhat, yhat, spread(nonempty[:, :], [P, J, D]), ALU.mult))
            v.scalar_tensor_tensor(out=xt[:, :, :], in0=yhat, scalar=0.0, in1=xt[:, :, :], op0=ALU.max,
                                   op1=ALU.add).then_inc(s_out, 1)


INPUTS = ["x", "src", "dst", "edge_type_86", "L0_gnn_attn_w", "L1_gnn_weight", "L1_gnn_w_comp",
          "L1_gnn_self_loop_weight", "L1_gnn_A1_w", "L1_gnn_A1_b", "L1_gnn_A2_w", "L1_gnn_A2_b", "L1_gnn_rel_emb"]


def kernel(**inputs):
    import concourse.bacc as bacc
    import numpy as np
    from concourse.bass_utils import run_bass_kernel_spmd

    nc = bacc.Bacc("TRN2", target_bir_lowering=False, num_devices=1)
    arrays, args = {}, []
    for name in INPUTS:
        a = np.ascontiguousarray(inputs[name])
        arrays[f"in_{name}"] = a
        args.append(nc.dram_tensor(f"in_{name}", a.shape, mybir.dt.from_np(a.dtype), kind="ExternalInput").ap())
    args.append(nc.dram_tensor("out_0", (N, D), fp32, kind="ExternalOutput").ap())
    build(nc, *args)
    r = run_bass_kernel_spmd(nc, [arrays], core_ids=[0])
    return r.results[0]["out_0"]
```
